# Optimizing a Trainium2 kernel written in Bass

```python
import numpy as np
import jax
import jax.numpy as jnp

def _softmax(x, axis=-1):
    return jax.nn.softmax(x, axis=axis)

def _gelu(x):
    return jax.nn.gelu(x, approximate=True)

def _silu(x):
    return jax.nn.silu(x)

def _sigmoid(x):
    return jax.nn.sigmoid(x)

def _layernorm(x, axis=-1, eps=1e-05):
    m = jnp.mean(x, axis=axis, keepdims=True)
    v = jnp.var(x, axis=axis, keepdims=True)
    return (x - m) / jnp.sqrt(v + eps)

def _scatter_add(tgt, idx, src, axis=0):
    return tgt.at[idx].add(src)

def _segment_sum(src, seg, n):
    return jax.ops.segment_sum(src, seg, n)
kernel_name = 'mk_gnn_ffn_d1_gnn_r8_d7cfa6'

def setup_inputs(seed: int=0):
    np.random.seed(seed)
    _w = jnp.asarray

    def _rec_inputs():
        import jax
        import jax.numpy as jnp
        _gk = jax.random.key(seed)
        x = -0.0001394 + 0.9999 * jax.random.normal(jax.random.fold_in(_gk, 1), (6250, 768), jnp.float32)
        _s = jax.random.randint(jax.random.fold_in(_gk, 2), (50000,), 0, 6250, jnp.int32)
        _d = jax.random.randint(jax.random.fold_in(_gk, 3), (50000,), 0, 6250, jnp.int32)
        _loop = jnp.arange(6250, dtype=jnp.int32)
        src = jnp.concatenate([_s, _d, _loop])
        dst = jnp.concatenate([_d, _s, _loop])
        _o = jnp.argsort(dst, stable=True)
        src = src[_o]
        dst = dst[_o]
        return (x, src, dst)
    x, src, dst = _rec_inputs()

    def _L0_gnn_setup():
        import jax, jax.numpy as jnp
        import numpy as np
        N_NODES = 6250

        def gcn_conv(x, edge_index, W, b, n_nodes):
            src = edge_index[0]
            dst = edge_index[1]
            loop = jnp.arange(n_nodes, dtype=src.dtype)
            src = jnp.concatenate([src, loop])
            dst = jnp.concatenate([dst, loop])
            deg = jax.ops.segment_sum(jnp.ones(src.shape, x.dtype), dst, num_segments=n_nodes)
            dinv = jnp.where(deg > 0, jax.lax.rsqrt(deg), jnp.zeros_like(deg))
            norm = dinv[src] * dinv[dst]
            h = x @ W.T
            msg = h[src] * norm[:, None]
            out = jax.ops.segment_sum(msg, dst, num_segments=n_nodes)
            return out + b
        key = jax.random.key(seed)
        k1, k2, k3, k4 = jax.random.split(key, 4)
        d = 768
        n_edges = 25000
        s = 1.0 / np.sqrt(d)
        return {'x': jax.random.normal(k1, (N_NODES, d), dtype=jnp.float32), 'edge_index': jax.random.randint(k2, (2, n_edges), 0, N_NODES, dtype=jnp.int64), 'W1': jax.random.normal(k3, (d, d), dtype=jnp.float32) * s, 'b1': jnp.zeros((d,), jnp.float32), 'W2': jax.random.normal(k4, (d, d), dtype=jnp.float32) * s, 'b2': jnp.zeros((d,), jnp.float32)}
    _L0_gnn_all = _L0_gnn_setup()
    _L0_gnn_in = {k: v for k, v in _L0_gnn_all.items() if k in ('W1', 'b1', 'W2', 'b2')}
    del _L0_gnn_all

    def _L0_ffn_setup():
        import jax, jax.numpy as jnp
        import numpy as np
        EPS = 1e-06

        def l2_normalize(x, axis):
            norm = jnp.sqrt(jnp.square(x).sum(axis=axis, keepdims=True))
            return x * (1.0 / (norm + EPS))
        key = jax.random.key(seed)
        ks = jax.random.split(key, 8)
        b, m, d = (32, 1024, 768)
        n, p = (8, 4)
        h = d // 8
        X = jax.random.normal(ks[0], (b, m, d), dtype=jnp.float32)
        std_slot = float(np.sqrt(2.0 / (d + n * p)))
        slot_params = jax.random.normal(ks[1], (d, n, p), dtype=jnp.float32) * std_slot
        scale = jnp.ones((), dtype=jnp.float32)
        W_down = jax.random.normal(ks[2], (n, d, h), dtype=jnp.float32) * float(np.sqrt(1.0 / d))
        b_down = jnp.zeros((n, h), dtype=jnp.float32)
        W_up = jax.random.normal(ks[3], (n, h, d), dtype=jnp.float32) * float(np.sqrt(1.0 / h))
        b_up = jnp.zeros((n, d), dtype=jnp.float32)
        return {'X': X, 'slot_params': slot_params, 'scale': scale, 'W_down': W_down, 'b_down': b_down, 'W_up': W_up, 'b_up': b_up}
    _L0_ffn_all = _L0_ffn_setup()
    _L0_ffn_in = {k: v for k, v in _L0_ffn_all.items() if k in ('slot_params', 'scale', 'W_down', 'b_down', 'W_up', 'b_up')}
    del _L0_ffn_all
    return {'x': x, 'src': src, 'dst': dst, 'L0_gnn_W1': _L0_gnn_in['W1'], 'L0_gnn_b1': _L0_gnn_in['b1'], 'L0_gnn_W2': _L0_gnn_in['W2'], 'L0_gnn_b2': _L0_gnn_in['b2'], 'L0_ffn_slot_params': _L0_ffn_in['slot_params'], 'L0_ffn_scale': _L0_ffn_in['scale'], 'L0_ffn_W_down': _L0_ffn_in['W_down'], 'L0_ffn_b_down': _L0_ffn_in['b_down'], 'L0_ffn_W_up': _L0_ffn_in['W_up'], 'L0_ffn_b_up': _L0_ffn_in['b_up']}

def reference(x, src, dst, L0_gnn_W1, L0_gnn_b1, L0_gnn_W2, L0_gnn_b2, L0_ffn_slot_params, L0_ffn_scale, L0_ffn_W_down, L0_ffn_b_down, L0_ffn_W_up, L0_ffn_b_up):
    import jax
    import jax.numpy as jnp

    def _L0_gnn_ref(x, edge_index, W1, b1, W2, b2):
        import jax, jax.numpy as jnp
        import numpy as np
        N_NODES = 6250

        def gcn_conv(x, edge_index, W, b, n_nodes):
            src = edge_index[0]
            dst = edge_index[1]
            loop = jnp.arange(n_nodes, dtype=src.dtype)
            src = jnp.concatenate([src, loop])
            dst = jnp.concatenate([dst, loop])
            deg = jax.ops.segment_sum(jnp.ones(src.shape, x.dtype), dst, num_segments=n_nodes)
            dinv = jnp.where(deg > 0, jax.lax.rsqrt(deg), jnp.zeros_like(deg))
            norm = dinv[src] * dinv[dst]
            h = x @ W.T
            msg = h[src] * norm[:, None]
            out = jax.ops.segment_sum(msg, dst, num_segments=n_nodes)
            return out + b
        h = gcn_conv(x, edge_index, W1, b1, N_NODES)
        h = jax.nn.relu(h)
        out = gcn_conv(h, edge_index, W2, b2, N_NODES)
        return out

    def _L0_ffn_ref(X, slot_params, scale, W_down, b_down, W_up, b_up):
        import jax, jax.numpy as jnp
        import numpy as np
        EPS = 1e-06

        def l2_normalize(x, axis):
            norm = jnp.sqrt(jnp.square(x).sum(axis=axis, keepdims=True))
            return x * (1.0 / (norm + EPS))
        b, m, d = X.shape
        _, n, p = slot_params.shape
        Xn = l2_normalize(X, axis=-1)
        sp = l2_normalize(slot_params, axis=1) * scale
        logits = jnp.einsum('bmd,dnp->bmnp', Xn, sp)
        D = jax.nn.softmax(logits, axis=1)
        C = jax.nn.softmax(logits.reshape(b, m, n * p), axis=2).reshape(b, m, n, p)
        X_tilde = jnp.einsum('bmd,bmnp->bnpd', Xn, D)
        H = jax.nn.gelu(jnp.einsum('bnpd,ndh->bnph', X_tilde, W_down) + b_down[None, :, None, :], approximate=False)
        Y_tilde = jnp.einsum('bnph,nhd->bnpd', H, W_up) + b_up[None, :, None, :]
        Y = jnp.einsum('bnpd,bmnp->bmd', Y_tilde, C)
        return Y
    edge_index = jnp.stack([src, dst])
    x = x + _L0_gnn_ref(_layernorm(x, axis=-1), edge_index, L0_gnn_W1, L0_gnn_b1, L0_gnn_W2, L0_gnn_b2)
    x = x + _L0_ffn_ref(_layernorm(x, axis=-1)[None], L0_ffn_slot_params, L0_ffn_scale, L0_ffn_W_down, L0_ffn_b_down, L0_ffn_W_up, L0_ffn_b_up)[0]
    return x

_drawn_inputs = setup_inputs


def setup_inputs(seed=0):
    import zlib

    import numpy as np

    out = dict(_drawn_inputs(seed))
    spreads = {'L0_gnn_b1': (0.0, 0.1),
     'L0_gnn_b2': (0.0, 0.1),
     'L0_ffn_b_down': (0.0, 0.451),
     'L0_ffn_b_up': (0.0, 0.1)}
    factors = {'L0_ffn_slot_params': 8.0, 'L0_ffn_W_down': 8.0, 'L0_ffn_W_up': 3.201}
    for name, (base, spread) in spreads.items():
        noise = np.random.default_rng([zlib.crc32(name.encode()), seed]).standard_normal(out[name].shape)
        drawn = base * np.exp(spread * noise) if base else spread * noise
        out[name] = jnp.asarray(drawn.astype(out[name].dtype))
    for name, factor in factors.items():
        out[name] = (out[name] * factor).astype(out[name].dtype)
    return out
```

```python
import numpy as np

N, D, E = 6250, 768, 106250
P = 128
T = -(-N // P)
LAST = N - (T - 1) * P
NPAD = T * P
KC = D // P
H = D // 2
PAIRS = 9
CHUNKS = 2 * PAIRS
WINDOW = CHUNKS * P
RING = 9
DEPTH = 3
EXPERTS, SLOTS_PER, HID = 8, 4, D // 8
SLOTS = EXPERTS * SLOTS_PER
EP = 125
EC = E // EP
GROUP = 17
GROUPS = EC // GROUP
PEELED = 5
CLEARS = 7
TC = T + 1
FAR = 16384.0
LN_EPS, L2_EPS = 1e-5, 1e-6


def build(nc, a):
    import concourse.bass as bass
    import concourse.mybir as mybir
    from contextlib import ExitStack

    f32, f32r, i32, bf16 = mybir.dt.float32, mybir.dt.float32r, mybir.dt.int32, mybir.dt.bfloat16
    ACT = mybir.ActivationFunctionType
    ALU = mybir.AluOpType
    AX = mybir.AxisListType
    ds = bass.ds
    ctx = ExitStack()
    with ctx:
        def sb(name, shape, dt=f32):
            return ctx.enter_context(nc.sbuf_tensor(name, shape, dt))

        def ps(name, shape, dt=f32):
            return ctx.enter_context(nc.psum_tensor(name, shape, dt))

        def sem(name):
            return ctx.enter_context(nc.semaphore(name))

        def dram(name, shape, dt=f32):
            return nc.dram_tensor(name, shape, dt, kind="Internal").ap()

        table = [dram("table_layer1", [2 * NPAD, D]), dram("table_layer2", [2 * NPAD, D])]
        xnew = dram("xnew", [NPAD, D])
        EPAD = E + WINDOW + P
        dst_pad, src_pad = (dram(n, [2 * EPAD], i32) for n in ("dst_pad", "src_pad"))

        ident = sb("ident", [P, P])
        ones = sb("ones", [P, P])
        iota_row = sb("iota_row", [P, P])
        tile_base = sb("tile_base", [P, T + 1])
        pad_edges = sb("pad_edges", [1, 2, WINDOW + P], i32)
        WT = [sb("WT1", [P, KC, D]), sb("WT2", [P, KC, D])]
        bias_bc = [sb("bias1", [P, D]), sb("bias2", [P, D])]
        dinv = sb("dinv", [P, TC])
        nmean = sb("nmean", [P, T])
        ssq = sb("ssq", [P, T])
        ssum = sb("ssum", [P, T])
        dump = sb("dump", [P, D], bf16)
        starts = sb("starts", [1, TC], i32)
        nleft = sb("nleft", [1, TC], i32)
        over = sb("over", [1, 2], i32)
        over_cols = sb("over_cols", [P, 2], i32)
        over_f = sb("over_f", [P, 5])
        over_idx = sb("over_idx", [P, 1], i32)
        sp_c = sb("sp_c", [P, KC, SLOTS])
        logits = sb("logits", [P, T, SLOTS])
        rows = sb("rows", [P, RING, 2, D])
        hi = sb("hi", [P, DEPTH, 2, D], f32r)
        lo = sb("lo", [P, DEPTH, 2, D], f32r)
        onehot = sb("onehot", [P, DEPTH, 2, P], f32r)
        erow = sb("erow", [64, P], i32)
        erow_f = sb("erow_f", [64, P])
        rel = sb("rel", [P, 2, CHUNKS])
        off = sb("off", [P, CHUNKS])
        gidx = sb("gidx", [P, 2, CHUNKS], i32)
        self_row = sb("self_row", [P, 2, D])
        agg = sb("agg", [P, D])
        aggT = sb("aggT", [P, KC, P])
        xs = sb("xs", [P, 2, D])
        xsT = sb("xsT", [P, KC, P])
        hid = sb("hid", [P, D])
        ynext = sb("ynext", [P, 2, D])
        small = sb("small", [P, 8, TC])
        bdown = sb("bdown", [EXPERTS, HID])
        bup = sb("bup", [EXPERTS, D])
        sel = sb("sel", [EXPERTS, EXPERTS, SLOTS_PER])
        hidT = sb("hidT", [HID, SLOTS])
        cT = sb("cT", [SLOTS, 2, P])
        w_tile = sb("w_tile", [P, 4, SLOTS])
        c_tile = sb("c_tile", [P, 2, SLOTS])

        acc = ps("acc", [P, 2, 2, 512])
        tp = ps("tp", [P, 2, 512])
        mm = ps("mm", [P, 2, 512])

        def halves(ap):
            return ap.rearrange("p (h n) -> p h n", h=2)

        class Steps:
            def __init__(self, eng, name):
                self.eng, self.sem, self.n = eng, sem(name), 0

            def mark(self, ins):
                self.n += 1
                ins.then_inc(self.sem, 1)
                return self.n

            def then(self, ins):
                self.mark(ins)
                self.eng.wait_ge(self.sem, self.n)

        s = {n: sem(n) for n in (
            "cleared", "ring_clear", "iotas", "flat_in", "pads_in", "misc_in", "ready_consts",
            "onehots_ready", "onehots_used", "x_read", "counts_sb", "degrees_done",
            "degrees_sb", "totals_done", "roots_ready",
            "coef_ready", "y_ready", "w_turned", "w_moved",
            "slots_scaled", "slot_sums", "slots_ready",
            "starts_ready", "x_step", "inv_ready")}
        s["w_in"] = [sem(f"w_in{b}") for b in range(2)]
        x_in = [sem(f"x_in{b}") for b in range(4)]
        y_out = [sem(f"y_out{b}") for b in range(4)]

        def load_sweep(eng, body):
            for t in range(5):
                body(0, t)
            trips = (T - 2) // 4
            with eng.Fori(1, trips) as i:
                for k in range(1, 5):
                    body(i, k)
            for t in range(trips * 4 + 1, T):
                body(0, t)

        def group_sweep(eng, body):
            for g in range(3):
                body(0, g)
            with eng.Fori(1, (GROUPS - 2) // 2) as i:
                for k in (1, 2):
                    body(i, k)
            body(0, GROUPS - 1)

        def layer_sweep(eng, body, before_loop=None):
            for t in range(PEELED):
                body(0, t)
            if before_loop:
                before_loop()
            with eng.Fori(PEELED // 2, (T - 1) // 2) as i:
                for k in (1, 2):
                    body(i, k)
            for t in (T, T + 1):
                body(0, t)

        def layer_sems(l):
            d = {n: sem(f"L{l}_{n}") for n in (
                "edges_in", "window_free", "edges_float", "edges_turned", "cols_step", "idx_ready",
                "hi_ready", "lo_ready", "pair_summed", "agg_ready", "agg_turned", "aggT_ready",
                "dense_done", "scaled_ready", "res_biased", "next_ready", "x_turned", "xT_ready", "logit_done",
                "logit_read", "mean_step", "stats_done")}
            for n in ("self_in", "res_in", "stored"):
                d[n] = [sem(f"L{l}_{n}{b}") for b in range(2)]
            return d
        L = [layer_sems(1), layer_sems(2)]
        rows_in = [sem(f"rows_in{b}") for b in range(RING)]
        F = {n: sem("F_" + n) for n in (
            "turned", "w_in", "w_staged", "c_staged", "mixed_done", "out_ready", "c_turned", "c_moved", "y_done",
            "exp_in", "exp_done", "root_in", "root_done", "gelu_in", "gelu_done", "top_ready", "sumd_ready", "sumd_done",
            "c_ready", "mix_ready", "mixT_ready", "down_done", "up_done", "yT_ready", "y_slots_ready")}
        fx_in = [sem(f"F_x_in{b}") for b in range(4)]
        f_out = [sem(f"F_out{b}") for b in range(4)]


        O = {n: sem("over_" + n) for n in (
            "dst_in", "src_in", "own_in", "own_out", "tile_added", "chunk_added", "wait_taken", "floated", "shifted",
            "clipped", "marked", "idx_ready", "rows_in", "hi_ready", "split", "summed")}

        def over_counters(eng, name):
            regs = [eng.alloc_register(f"{name}_{n}") for n in ("chunk", "chunk16", "tile", "tile16")]
            for reg, v in zip(regs, (1, 16, 1, 16)):
                eng.reg_mov(reg, v)
            return regs

        def over_loops(eng, per_chunk, before_chunks=None, after_chunks=None):
            tiles = eng.value_load(over[0:1, 0:1], min_val=0, max_val=T)
            with eng.Fori(0, tiles) as t:
                if before_chunks:
                    before_chunks(t)
                chunks = eng.value_load(nleft[0:1, ds(t, 1)], min_val=0, max_val=E // P + 1)
                with eng.Fori(0, chunks) as i:
                    per_chunk(t, i)
                if after_chunks:
                    after_chunks(t)

        def over_sp(sp, l, nth, nth16, tile, tile16):

            def own_rows(t):
                sp.dma_start(agg[:, :], table[l][ds(t * P, P), :]).then_inc(O["own_in"], 16)

            def chunk(t, i):
                first = sp.value_load(starts[0:1, ds(t, 1)], min_val=0, max_val=E)
                sp.wait_ge(O["chunk_added"], nth)
                sp.sem_inc(O["wait_taken"], 1)
                sp.reg_add(nth, nth, 1)
                for col, pad, done in ((0, dst_pad, "dst_in"), (1, src_pad, "src_in")):
                    sp.dma_start(over_cols[:, col:col + 1],
                                 pad[ds(first + i * P + WINDOW, P)].rearrange("(p c) -> p c", c=1)
                                 ).then_inc(O[done], 16)

            def store(t):
                sp.wait_ge(O["tile_added"], tile)
                sp.sem_inc(O["wait_taken"], 1)
                sp.dma_start(table[l][ds(t * P + NPAD, P), :], agg[:, :]).then_inc(O["own_out"], 16)
                sp.wait_ge(O["own_out"], tile16)
                sp.sem_inc(O["wait_taken"], 1)
                sp.reg_add(tile, tile, 1)
                sp.reg_add(tile16, tile16, 16)
            over_loops(sp, chunk, own_rows, store)

        def over_dve(dve, l, nth, nth16, tile, tile16):
            if l == 0:
                dve.sem_inc(O["chunk_added"], 1)

            def chunk(t, i):
                dve.wait_ge(O["dst_in"], nth16)
                dve.wait_ge(O["src_in"], nth16)
                dve.tensor_copy(over_f[:, 0:2], over_cols[:, :]).then_inc(O["floated"], 1)
                dve.wait_ge(O["floated"], nth)
                dve.tensor_scalar(over_f[:, 2:3], over_f[:, 0:1], tile_base[:, ds(t, 1)], None, ALU.subtract
                                  ).then_inc(O["shifted"], 1)
                dve.wait_ge(O["shifted"], nth)
                dve.tensor_scalar(over_f[:, 3:4], over_f[:, 2:3], 0.0, P - 1.0, ALU.max, ALU.min).then_inc(O["clipped"], 1)
                dve.wait_ge(O["clipped"], nth)
                dve.tensor_tensor(over_f[:, 4:5], over_f[:, 3:4], over_f[:, 2:3], ALU.not_equal).then_inc(O["marked"], 1)
                dve.wait_ge(O["marked"], nth)
                dve.tensor_scalar(onehot[:, 0, 0, :], iota_row[:, :], over_f[:, 2:3], None, ALU.is_equal)
                dve.scalar_tensor_tensor(over_idx[:, :], over_f[:, 4:5], FAR, over_f[:, 1:2], ALU.mult, ALU.add
                                         ).then_inc(O["idx_ready"], 1)
                dve.wait_ge(O["rows_in"], nth16)
                dve.tensor_copy(hi[:, 0, 0, :], rows[:, 0, 0, :]).then_inc(O["hi_ready"], 1)
                dve.wait_ge(O["hi_ready"], nth)
                dve.tensor_tensor(lo[:, 0, 0, :], rows[:, 0, 0, :], hi[:, 0, 0, :].bitcast(f32), ALU.subtract
                                  ).then_inc(O["split"], 1)
                dve.wait_ge(O["own_in"], tile16)
                dve.wait_ge(O["summed"], nth)
                dve.tensor_tensor(halves(agg[:, :]), acc[:, 0, :, 0:H], halves(agg[:, :]), ALU.add
                                  ).then_inc(O["chunk_added"], 1)
                dve.reg_add(nth, nth, 1)
                dve.reg_add(nth16, nth16, 16)
                dve.wait_ge(O["chunk_added"], nth)

            def done(t):
                dve.wait_ge(O["own_in"], tile16)
                dve.sem_inc(O["tile_added"], 1)
                dve.reg_add(tile, tile, 1)
                dve.reg_add(tile16, tile16, 16)
            over_loops(dve, chunk, None, done)

        def over_pool(pool, l, bound, nth, nth16, tile, tile16):

            def chunk(t, i):
                pool.wait_ge(O["idx_ready"], nth)
                pool.sem_inc(O["wait_taken"], 1)
                pool.indirect_dma_start(rows[:, 0, 0, :], None, table[l][0:N, :],
                                        bass.IndirectOffsetOnAxis(ap=over_idx[:, 0:1], axis=0),
                                        bounds_check=bound, oob_is_err=False).then_inc(O["rows_in"], 16)
                pool.wait_ge(O["summed"], nth)
                pool.reg_add(nth, nth, 1)
            over_loops(pool, chunk)

        def over_pe(pe, l, nth, nth16, tile, tile16):

            def chunk(t, i):
                pe.wait_ge(O["split"], nth)
                for part in (hi, lo):
                    for h in range(2):
                        m = pe.matmul(acc[:, 0, h, 0:H], onehot[:, 0, 0, :], part[:, 0, 0, h * H:(h + 1) * H],
                                      start=part is hi, stop=part is lo)
                m.then_inc(O["summed"], 1)
                pe.reg_add(nth, nth, 1)
            over_loops(pe, chunk)

        flat = rows[:, :, :, :].rearrange("p a b d -> p (a b d)")
        arena = flat[:, 7 * EC:]
        xin = arena[:, 0:4 * D].rearrange("p (b d) -> p b d", b=4)
        oh_low = arena[:, 4 * D:4 * D + GROUP * P].bitcast(bf16).rearrange(
            "p (b j r) -> p b j r", b=2, j=GROUP)
        hist0 = 4 * D + GROUP * P
        oh_high = arena[:, hist0:hist0 + GROUP * T].bitcast(bf16).rearrange(
            "p (b j r) -> p b j r", b=2, j=GROUP)
        iota_b = xs[:, 0, 0:P // 2].bitcast(bf16)
        d_flat = flat[0:EP, 0:EC].bitcast(i32)
        dn_flat = flat[0:EP, EC:2 * EC].bitcast(i32)
        d_high_i = flat[0:EP, 2 * EC:3 * EC].bitcast(i32)
        d_low_i = flat[0:EP, 3 * EC:4 * EC].bitcast(i32)
        d_high = flat[0:EP, 4 * EC:5 * EC]
        d_low = flat[0:EP, 5 * EC:6 * EC]
        viol = flat[0:EP, 6 * EC:7 * EC]

        def done_count(k0, n):
            return 16 * len(range(k0, T, n))

        def full(i, k, t):
            return LAST if isinstance(i, int) and t == T - 1 else P

        deg, recip_deg, recip_var, norm2 = (small[:, j, :] for j in range(4))
        norm2_kq = norm2[:, 0:KC * SLOTS_PER].rearrange("p (k q) -> p k q", k=KC)
        coef, shift, scale_col, vsum = small[:, 4, 0:T], small[:, 5, 0:T], small[:, 6, 0:1], small[0:EP, 6, 1:2]
        tot, incl, ends = small[0:1, 7, :], agg[0:1, 0:TC], agg[0:1, 64:64 + TC]
        is_sorted, any_over = agg[0:1, 128:129], agg[0:1, 129:130]
        ffn = flat[:, 4 * D + T * SLOTS:]
        wdown = WT[0][:, :, :].rearrange("p k (n h) -> p k n h", n=EXPERTS)
        wup = ffn[0:HID, 0:EXPERTS * D].rearrange("p (n d) -> p n d", n=EXPERTS)
        cw = ffn[:, EXPERTS * D:EXPERTS * D + T * SLOTS].rearrange("p (t q) -> p t q", t=T)
        xr = flat[:, 0:4 * D].rearrange("p (b d) -> p b d", b=4)
        dw = flat[:, 4 * D:4 * D + T * SLOTS].rearrange("p (t q) -> p t q", t=T)

        block = ctx.enter_context(nc.Block())

        @block.sync
        def _(sp):
            sp.wait_ge(s["cleared"], 2)
            sp.dma_start(d_flat, a["dst"].rearrange("(p c) -> p c", p=EP)).then_inc(s["flat_in"], 16)
            sp.dma_start(dn_flat[0:EP - 1, :],
                         a["dst"][1:1 + (EP - 1) * EC].rearrange("(p c) -> p c", p=EP - 1)).then_inc(s["flat_in"], 16)
            sp.dma_start(dn_flat[EP - 1:EP, 0:EC - 1],
                         a["dst"][1 + (EP - 1) * EC:E].rearrange("(p c) -> p c", p=1)).then_inc(s["flat_in"], 16)
            for l, name in ((0, "W1"), (1, "W2")):
                for o in range(KC):
                    n = l * KC + o
                    if n >= 2:
                        sp.wait_ge(s["w_turned"], n - 1)
                    sp.dma_start(ynext[:, n % 2, :], a[name][o * P:(o + 1) * P, :]).then_inc(s["w_in"][n % 2], 16)

            def load_x(i, k):
                t, b = 4 * i + k, k % 4
                if k >= 4 or not isinstance(i, int):
                    sp.wait_ge(s["x_read"], t - 3)
                n = full(i, k, t)
                sp.dma_start(xin[0:n, b, :], a["x"][ds(t * P, n), :]).then_inc(x_in[b], 16)
            sp.wait_ge(s["ring_clear"], 1)
            load_sweep(sp, load_x)
            sp.wait_ge(s["cleared"], CLEARS)
            sp.dma_start(dst_pad[0:E].rearrange("(p c) -> p c", p=EP),
                         a["dst"].rearrange("(p c) -> p c", p=EP)).then_inc(s["pads_in"], 16)
            sp.dma_start(src_pad[0:E].rearrange("(p c) -> p c", p=EP),
                         a["src"].rearrange("(p c) -> p c", p=EP)).then_inc(s["pads_in"], 16)
            sp.dma_start(dst_pad[E:EPAD].rearrange("(p c) -> p c", p=1), pad_edges[0:1, 0, :]).then_inc(s["pads_in"], 16)
            sp.dma_start(src_pad[E:EPAD].rearrange("(p c) -> p c", p=1), pad_edges[0:1, 1, :]).then_inc(s["pads_in"], 16)
            for dst_ap, src_ap in ((bias_bc[0][:, :], a["b1"].partition_broadcast(P)),
                                   (bias_bc[1][:, :], a["b2"].partition_broadcast(P)),
                                   (sp_c[:, :, :], a["slots"].rearrange("(k p) n q -> p k (n q)", p=P)),
                                   (scale_col, a["scale"].partition_broadcast(P))):
                sp.dma_start(dst_ap, src_ap).then_inc(s["misc_in"], 16)

            def reload_x(i, k):
                t, b = 4 * i + k, k % 4
                if k >= 4 or not isinstance(i, int):
                    sp.wait_ge(y_out[b], 16 * (i + k // 4))
                else:
                    sp.wait_ge(s["x_read"], T)
                n = full(i, k, t)
                sp.dma_start(xin[0:n, b, :], a["x"][ds(t * P, n), :]).then_inc(x_in[b], 16)
            load_sweep(sp, reload_x)

            sp.wait_ge(s["pads_in"], 64)
            sp.wait_ge(s["starts_ready"], 1)
            counts = over_counters(sp, "sp")
            for l in range(2):
                S = L[l]
                if l == 1:
                    sp.wait_ge(L[0]["edges_float"], T + 1)

                def load_edges(t):
                    first = sp.value_load(starts[0:1, ds(t, 1)], min_val=0, max_val=E)
                    if not (isinstance(t, int) and t == 0):
                        sp.wait_ge(S["edges_float"], t)
                        sp.sem_inc(S["window_free"], 1)
                    for row, pad in ((0, dst_pad), (32, src_pad)):
                        sp.dma_start(erow[row:row + CHUNKS, :],
                                     pad[ds(first, WINDOW)].rearrange("(c p) -> c p", p=P)).then_inc(S["edges_in"], 16)

                load_edges(0)
                for b in range(4 if l == 0 else 2):
                    sp.wait_ge(y_out[b] if l == 0 else L[0]["stored"][b], done_count(b, 4 if l == 0 else 2))
                over_sp(sp, l, *counts)
                own_rows = sp.value_load(over[0:1, 1:2], min_val=0, max_val=NPAD)

                def step(i, k):
                    t = 2 * i + k
                    known = isinstance(i, int)
                    if not (known and t >= T):
                        load_edges(t + 1)
                        if not known or t >= 2:
                            sp.wait_ge(S["agg_ready"], t - 1)
                        sp.dma_start(self_row[:, k % 2, :], table[l][ds(own_rows + t * P, P), :]).then_inc(S["self_in"][k % 2], 16)
                    if l == 1 and not (known and (t < 1 or t > T)):
                        b = (k - 1) % 2
                        if not known or t >= 3:
                            sp.wait_ge(S["stats_done"], t - 2)
                            sp.wait_ge(S["x_turned"], t - 2)
                            sp.sem_inc(S["window_free"], 1)
                            sp.wait_ge(S["stored"][b], 16 * (i + (k - 3) // 2 + 1))
                        n = LAST if known and t == T else P
                        sp.dma_start(xs[0:n, b, :], a["x"][ds((t - 1) * P, n), :]).then_inc(S["res_in"][b], 16)
                    if not (known and t < 2):
                        out, src = (table[1], ynext) if l == 0 else (xnew, xs)
                        sp.wait_ge(S["next_ready"], t - 1)
                        sp.dma_start(out[ds((t - 2) * P, P), :], src[:, k % 2, :]).then_inc(S["stored"][k % 2], 16)
                layer_sweep(sp, step)
                if l == 0:
                    for b in range(2):
                        sp.wait_ge(L[0]["stored"][b], done_count(b, 2))
                    for n in range(EXPERTS):
                        sp.dma_start(wdown[:, :, n, :], a["W_down"][n].rearrange("(k p) h -> p k h", p=P)
                                     ).then_inc(F["w_in"], 16)
                    sp.dma_start(bdown[:, :], a["b_down"]).then_inc(F["w_in"], 16)
                    sp.dma_start(bup[:, :], a["b_up"]).then_inc(F["w_in"], 16)

            for b in range(2):
                sp.wait_ge(L[1]["stored"][b], done_count(b, 2))
            sp.dma_start(wup, a["W_up"].rearrange("n h d -> h n d")).then_inc(F["w_in"], 16)

            def load_mix(i, k):
                t, b = 4 * i + k, k % 4
                if k >= 4 or not isinstance(i, int):
                    sp.wait_ge(F["mixed_done"], t - 3)
                sp.dma_start(xr[:, b, :], xnew[ds(t * P, P), :]).then_inc(fx_in[b], 16)
            load_sweep(sp, load_mix)

            def load_out(i, k):
                t, b = 4 * i + k, k % 4
                if k >= 4 or not isinstance(i, int):
                    sp.wait_ge(f_out[b], 16 * (i + k // 4))
                else:
                    sp.wait_ge(F["mixed_done"], T)
                sp.dma_start(xr[:, b, :], xnew[ds(t * P, P), :]).then_inc(fx_in[b], 16)
            load_sweep(sp, load_out)
            for b in range(4):
                sp.wait_ge(f_out[b], done_count(b, 4))

        @block.gpsimd
        def _(pool):
            pool.memset(flat[:, 0:2 * EC], 0.0).then_inc(s["cleared"], 1)
            pool.wait_ge(s["cleared"], 1)
            pool.memset(dn_flat[:, EC - 1:EC], N).then_inc(s["cleared"], 1)
            for ap, v in ((ident[:, :], 0.0), (ones[:, :], 1.0), (pad_edges[:, 0, :], -1), (pad_edges[:, 1, :], 0),
                          (erow[:, :], 0)):
                pool.memset(ap, v).then_inc(s["cleared"], 1)
            pool.iota(iota_row[:, :], pattern=[[1, P]], base=0, channel_multiplier=0,
                      allow_small_or_imprecise_dtypes=True).then_inc(s["iotas"], 1)
            pool.iota(tile_base[:, :], pattern=[[P, T + 1]], base=0, channel_multiplier=0,
                      allow_small_or_imprecise_dtypes=True).then_inc(s["iotas"], 1)
            pool.iota(iota_b[:, :], pattern=[[1, P]], base=0, channel_multiplier=0,
                      allow_small_or_imprecise_dtypes=True).then_inc(s["iotas"], 1)
            pool.wait_ge(s["cleared"], CLEARS)
            pool.affine_select(out=ident[:, :], in_=ident[:, :], compare_op=ALU.not_equal, fill=1.0,
                               base=0, pattern=[[-1, P]], channel_multiplier=1).then_inc(s["ready_consts"], 1)
            for b in range(4):
                pool.wait_ge(y_out[b], done_count(b, 4))
            bound = pool.to_reg(N - 1)
            counts = over_counters(pool, "pool")
            idx_needed, lo_needed = pool.alloc_register("idx_needed"), pool.alloc_register("lo_needed")
            for l in range(2):
                S = L[l]
                if l == 1:
                    for b in range(2):
                        pool.wait_ge(L[0]["stored"][b], done_count(b, 2))

                over_pool(pool, l, bound, *counts)

                def counters():
                    pool.reg_mov(idx_needed, PEELED + 1)
                    pool.reg_mov(lo_needed, PAIRS * PEELED - RING + 1)

                def step(i, k):
                    t = 2 * i + k
                    known = isinstance(i, int)
                    if known and t >= T:
                        return
                    for j in range(PAIRS):
                        slot = (PAIRS * k + j) % RING
                        if j == 0:
                            if known:
                                pool.wait_ge(S["idx_ready"], t + 1)
                            else:
                                pool.wait_ge(S["idx_ready"], idx_needed)
                                pool.reg_add(idx_needed, idx_needed, 1)
                        if not known:
                            pool.wait_ge(S["lo_ready"], lo_needed)
                            pool.reg_add(lo_needed, lo_needed, 1)
                        elif PAIRS * t + j >= RING:
                            pool.wait_ge(S["lo_ready"], PAIRS * t + j - RING + 1)
                        for c in range(2):
                            pool.indirect_dma_start(
                                rows[:, slot, c, :], None, table[l][0:N, :],
                                bass.IndirectOffsetOnAxis(ap=gidx[:, k % 2, 2 * j + c:2 * j + c + 1], axis=0),
                                bounds_check=bound, oob_is_err=False).then_inc(rows_in[slot], 16)
                layer_sweep(pool, step, counters)

        @block.scalar
        def _(act):
            for n in range(2 * KC):
                l, o = divmod(n, KC)
                act.wait_ge(s["w_turned"], n + 1)
                act.activation(WT[l][:, :, o * P:(o + 1) * P].rearrange("p (h k) n -> p h k n", h=2),
                               tp[:, :, 0:H].rearrange("p h (k n) -> p h k n", k=KC // 2), ACT.Copy
                               ).then_inc(s["w_moved"], 1)

            def measure(rows_ap, t, step_sem, read_sem):
                act.activation(dump[:, :], rows_ap, ACT.Copy, accum_out=ssum[:, ds(t, 1)]).then_inc(step_sem, 1)
                act.wait_ge(step_sem, 2 * t + 1)
                act.activation(nmean[:, ds(t, 1)], ssum[:, ds(t, 1)], ACT.Copy, scale=-1.0 / D).then_inc(step_sem, 1)
                act.wait_ge(step_sem, 2 * t + 2)
                act.activation(dump[:, :], rows_ap, ACT.Square, bias=nmean[:, ds(t, 1)],
                               accum_out=ssq[:, ds(t, 1)]).then_inc(read_sem, 1)

            def stats(i, k):
                t, b = 4 * i + k, k % 4
                if not (isinstance(i, int) and t == 0):
                    act.wait_ge(s["x_read"], t)
                act.wait_ge(x_in[b], 16 * (i + k // 4 + 1))
                measure(xin[:, b, :], t, s["x_step"], s["x_read"])
            load_sweep(act, stats)
            act.wait_ge(s["inv_ready"], 1)
            for ap in (recip_deg, recip_var[:, 0:T], norm2[:, 0:KC * SLOTS_PER]):
                act.activation(ap, ap, ACT.Sqrt).then_inc(s["roots_ready"], 1)

            def store_y(i, k):
                t, b = 4 * i + k, k % 4
                act.wait_ge(s["y_ready"], t + 1)
                act.dma_start(table[0][ds(t * P, P), :], xin[:, b, :]).then_inc(y_out[b], 16)
            load_sweep(act, store_y)

            for l in range(2):
                S = L[l]
                if l == 1:
                    for b in range(2):
                        act.wait_ge(L[0]["stored"][b], done_count(b, 2))

                def step(i, k):
                    t = 2 * i + k
                    known = isinstance(i, int)
                    pairs, stage_a, stage_b = (not known or t < T), (not known or 1 <= t <= T), (not known or t >= 2)
                    for j in range(PAIRS):
                        if pairs:
                            g, slot, pb = PAIRS * t + j, (PAIRS * k + j) % RING, (PAIRS * k + j) % DEPTH
                            before = l * len(range(slot, PAIRS * T, RING))
                            act.wait_ge(rows_in[slot],
                                        32 * (2 * PAIRS // RING * i + (PAIRS * k + j) // RING + 1 + before))
                            if not known or g >= DEPTH:
                                act.wait_ge(S["pair_summed"], g - DEPTH + 1)
                            act.activation(hi[:, pb, :, :], rows[:, slot, :, :], ACT.Copy).then_inc(S["hi_ready"], 1)
                        if j == 7 and l == 0 and stage_b:
                            act.wait_ge(S["scaled_ready"], t - 1)
                            if not known or t >= 4:
                                act.wait_ge(S["stored"][k % 2], 16 * (i + (k - 4) // 2 + 1))
                            act.activation(ynext[:, k % 2, :], hid[:, :], ACT.Relu,
                                           scale=dinv[:, ds(t - 2, 1)]).then_inc(S["next_ready"], 1)
                        if j == 5 and stage_a:
                            act.wait_ge(S["agg_turned"], t)
                            if not known or t >= 2:
                                act.wait_ge(S["dense_done"], t - 1)
                            act.activation(halves(aggT[:, :, :].rearrange("p k n -> p (k n)")), tp[:, :, 0:H],
                                           ACT.Copy).then_inc(S["aggT_ready"], 1)
                        if j == 7 and l == 1 and stage_b:
                            if not known or t >= 3:
                                act.wait_ge(S["stats_done"], t - 2)
                            act.wait_ge(S["next_ready"], t - 1)
                            measure(xs[:, k % 2, :], t - 2, S["mean_step"], S["stats_done"])
                        if j == 8 and l == 1 and stage_b:
                            act.wait_ge(S["x_turned"], t - 1)
                            if not known or t >= 3:
                                act.wait_ge(S["logit_done"], t - 2)
                            act.activation(halves(xsT[:, :, :].rearrange("p k n -> p (k n)")), tp[:, :, 0:H],
                                           ACT.Copy).then_inc(S["xT_ready"], 1)
                layer_sweep(act, step)

            act.wait_ge(F["root_in"], 1)
            act.activation(recip_var[:, 0:T], recip_var[:, 0:T], ACT.Sqrt).then_inc(F["root_done"], 1)
            act.activation(coef, coef, ACT.Sqrt).then_inc(F["root_done"], 1)
            act.wait_ge(F["exp_in"], 1)
            act.activation(dw[:, :, :], dw[:, :, :], ACT.Exp).then_inc(F["exp_done"], 1)
            act.wait_ge(F["exp_in"], 2)
            act.activation(cw[:, :, :], cw[:, :, :], ACT.Exp).then_inc(F["exp_done"], 1)

            def stage_w(i, k):
                t = 4 * i + k
                if k >= 4 or not isinstance(i, int):
                    act.wait_ge(F["mixed_done"], t - 3)
                act.activation(w_tile[:, k % 4, :], dw[:, ds(t, 1), :], ACT.Copy, scale=coef[:, ds(t, 1)]
                               ).then_inc(F["w_staged"], 1)
            act.wait_ge(F["exp_done"], 1)
            load_sweep(act, stage_w)
            act.wait_ge(F["gelu_in"], 1)
            act.activation(hidT[:, :], hidT[:, :], ACT.Gelu).then_inc(F["gelu_done"], 1)

            def stage_c(t, b):
                act.activation(c_tile[:, b, :], cw[:, ds(t, 1), :], ACT.Copy).then_inc(F["c_staged"], 1)
            act.wait_ge(F["c_ready"], 1)
            stage_c(0, 0)
            stage_c(1, 1)

            def move_c(i, k):
                t = 4 * i + k
                act.wait_ge(F["c_turned"], t + 1)
                if k >= 2 or not isinstance(i, int):
                    act.wait_ge(F["y_done"], t - 1)
                act.activation(cT[:, k % 2, :], tp[0:SLOTS, k % 2, 0:P], ACT.Copy).then_inc(F["c_moved"], 1)
                if not (isinstance(i, int) and t >= T - 2):
                    stage_c(t + 2, k % 2)
                if not (isinstance(i, int) and t == 0):
                    store_out(t - 1, (k - 1) % 4, P)

            def store_out(t, b, n):
                act.wait_ge(F["out_ready"], t + 1)
                act.dma_start(a["out"][ds(t * P, n), :], xr[0:n, b, :]).then_inc(f_out[b], 16)
            load_sweep(act, move_c)
            store_out(T - 1, (T - 1) % 4, LAST)

        @block.vector
        def _(dve):
            one = Steps(dve, "dve_step")
            dve.memset(flat[:, 2 * EC:], 0.0).then_inc(s["ring_clear"], 1)
            dve.wait_ge(s["ring_clear"], 1)
            dve.wait_ge(s["flat_in"], 48)
            one.mark(dve.tensor_scalar(d_high_i, d_flat, 7, None, ALU.arith_shift_right))
            one.mark(dve.tensor_scalar(d_low_i, d_flat, P - 1, None, ALU.bitwise_and))
            one.then(dve.tensor_tensor(viol, dn_flat, d_flat, ALU.is_lt))
            one.mark(dve.tensor_copy(d_high, d_high_i))
            one.mark(dve.tensor_copy(d_low, d_low_i))
            one.then(dve.tensor_reduce(vsum, viol, AX.X, ALU.add))
            dve.wait_ge(s["iotas"], 3)

            def onehots(i, k):
                b, g = k % 2, 2 * i + k
                if k >= 2 or not isinstance(i, int):
                    dve.wait_ge(s["onehots_used"], g - 1)
                dve.tensor_tensor(oh_low[0:EP, b, :, :], iota_b[0:EP, :].unsqueeze(1).to_broadcast([EP, GROUP, P]),
                                  d_low[:, ds(g * GROUP, GROUP)].unsqueeze(2).to_broadcast([EP, GROUP, P]), ALU.is_equal)
                dve.tensor_tensor(oh_high[0:EP, b, :, :], iota_row[0:EP, 0:T].unsqueeze(1).to_broadcast([EP, GROUP, T]),
                                  d_high[:, ds(g * GROUP, GROUP)].unsqueeze(2).to_broadcast([EP, GROUP, T]),
                                  ALU.is_equal).then_inc(s["onehots_ready"], 1)
            group_sweep(dve, onehots)
            dve.wait_ge(s["onehots_used"], GROUPS)
            dve.tensor_copy(hid[0:T, 0:P], mm[0:T, 0, 0:P]).then_inc(s["counts_sb"], 1)
            one.mark(dve.memset(deg[:, T:TC], 0.0))
            dve.wait_ge(s["degrees_done"], 1)
            one.then(dve.tensor_copy(deg[:, 0:T], tp[:, 0, 0:T]))
            dve.sem_inc(s["degrees_sb"], 1)
            dve.wait_ge(s["totals_done"], 1)
            one.mark(dve.tensor_copy(tot, tp[0:1, 1, 0:TC]))
            one.then(dve.tensor_scalar(is_sorted, tp[0:1, 1, 64:65], 0.0, None, ALU.is_equal))
            one.then(dve.tensor_tensor_scan(incl, ones[0:1, 0:TC], tot, 0.0, ALU.mult, ALU.add))
            one.then(dve.tensor_tensor(tot, incl, tot, ALU.subtract))
            one.mark(dve.tensor_scalar(tot, tot, is_sorted, None, ALU.mult))
            one.then(dve.tensor_scalar(ends, incl, float(E), is_sorted, ALU.subtract, ALU.mult))
            one.then(dve.tensor_scalar(ends, ends, float(E), None, ALU.add))
            one.mark(dve.tensor_copy(starts[:, :], tot))
            one.then(dve.tensor_tensor(ends, ends, tot, ALU.subtract))
            one.then(dve.tensor_scalar(ends, ends, float(P - 1 - WINDOW), 0.0, ALU.add, ALU.max))
            one.then(dve.tensor_copy(nleft[:, :], ends))
            one.then(dve.tensor_scalar(nleft[:, :], nleft[:, :], 7, None, ALU.arith_shift_right))
            one.then(dve.tensor_copy(ends, nleft[:, :]))
            one.then(dve.tensor_reduce(any_over, ends, AX.X, ALU.max))
            one.mark(dve.tensor_scalar(over[:, 0:1], any_over, 0.0, float(T), ALU.is_gt, ALU.mult))
            one.then(dve.tensor_scalar(over[:, 1:2], any_over, 0.0, float(NPAD), ALU.is_gt, ALU.mult))
            one.eng.sem_inc(s["starts_ready"], 1)
            dve.wait_ge(s["misc_in"], 64)
            one.then(dve.tensor_tensor(aggT[:, :, 0:SLOTS], sp_c[:, :, :], sp_c[:, :, :], ALU.mult))
            one.mark(dve.tensor_reduce(norm2_kq, aggT[:, :, 0:SLOTS].rearrange("p k (n q) -> p k q n", n=EXPERTS),
                                       AX.X, ALU.add))
            one.then(dve.tensor_scalar(deg, deg, 1.0, None, ALU.add))
            one.mark(dve.reciprocal(recip_deg, deg))
            dve.wait_ge(s["x_read"], T)
            one.then(dve.tensor_scalar(recip_var[:, 0:T], ssq[:, :], 1.0 / D, LN_EPS, ALU.mult, ALU.add))
            one.mark(dve.reciprocal(recip_var[:, 0:T], recip_var[:, 0:T]))
            dve.wait_ge(one.sem, one.n)
            one.eng.sem_inc(s["inv_ready"], 1)
            dve.wait_ge(s["roots_ready"], 3)
            one.mark(dve.tensor_copy(dinv[:, :], recip_deg))
            one.mark(dve.tensor_scalar(norm2_kq, norm2_kq, L2_EPS, None, ALU.add))
            one.then(dve.tensor_tensor(coef, recip_var[:, 0:T], recip_deg[:, 0:T], ALU.mult))
            one.mark(dve.tensor_tensor(shift, nmean[:, :], coef, ALU.mult))
            one.then(dve.reciprocal(norm2_kq, norm2_kq))
            one.then(dve.tensor_scalar(norm2_kq, norm2_kq, scale_col, None, ALU.mult))
            for n in range(EXPERTS):
                q = slice(n * SLOTS_PER, (n + 1) * SLOTS_PER)
                one.mark(dve.tensor_tensor(sp_c[:, :, q], sp_c[:, :, q], norm2_kq, ALU.mult))
            dve.wait_ge(one.sem, one.n)
            dve.sem_inc(s["slots_scaled"], 1)

            def scale_x(i, k):
                t, b = 4 * i + k, k % 4
                dve.wait_ge(x_in[b], 16 * (i + k // 4 + 1) + done_count(b, 4))
                dve.tensor_scalar(xin[:, b, :], xin[:, b, :], coef[:, ds(t, 1)], shift[:, ds(t, 1)],
                                  ALU.mult, ALU.add).then_inc(s["y_ready"], 1)
            load_sweep(dve, scale_x)
            dve.wait_ge(s["slot_sums"], 1)
            one.then(dve.tensor_scalar(norm2[:, 0:SLOTS], mm[:, 1, 0:SLOTS], 1.0 / D, None, ALU.mult))
            one.then(dve.tensor_tensor(sp_c[:, :, :], sp_c[:, :, :],
                                       norm2[:, 0:SLOTS].unsqueeze(1).to_broadcast([P, KC, SLOTS]), ALU.subtract))
            one.eng.sem_inc(s["slots_ready"], 1)

            counts = over_counters(dve, "dve")
            for l in range(2):
                S = L[l]

                def window_float(t):
                    dve.wait_ge(S["edges_in"], 32 * (t + 1))
                    if not (isinstance(t, int) and t == 0):
                        dve.wait_ge(S["edges_turned"], t)
                    dve.tensor_copy(erow_f[0:32 + CHUNKS, :], erow[0:32 + CHUNKS, :]).then_inc(S["edges_float"], 1)

                def window_cols(t, b):
                    dve.wait_ge(S["edges_turned"], t + 1)
                    c = S["cols_step"]
                    dve.tensor_scalar(rel[:, b, :], tp[:, 0, H:H + CHUNKS], tile_base[:, ds(t, 1)], None,
                                      ALU.subtract).then_inc(c, 1)
                    dve.wait_ge(c, 3 * t + 1)
                    dve.tensor_scalar(off[:, :], rel[:, b, :], 0.0, P - 1.0, ALU.max, ALU.min).then_inc(c, 1)
                    dve.wait_ge(c, 3 * t + 2)
                    dve.tensor_tensor(off[:, :], off[:, :], rel[:, b, :], ALU.not_equal).then_inc(c, 1)
                    dve.wait_ge(c, 3 * t + 3)
                    dve.scalar_tensor_tensor(gidx[:, b, :], off[:, :], FAR, tp[:, 0, H + 32:H + 32 + CHUNKS],
                                             ALU.mult, ALU.add).then_inc(S["idx_ready"], 1)

                window_float(0)
                window_cols(0, 0)
                if l == 1:
                    for b in range(2):
                        dve.wait_ge(L[0]["stored"][b], done_count(b, 2))
                over_dve(dve, l, *counts)

                def step(i, k):
                    t = 2 * i + k
                    known = isinstance(i, int)
                    pairs, stage_a, stage_b = (not known or t < T), (not known or 1 <= t <= T), (not known or t >= 2)
                    for j in range(PAIRS):
                        if pairs:
                            g, slot, pb = PAIRS * t + j, (PAIRS * k + j) % RING, (PAIRS * k + j) % DEPTH
                            if not known or g >= DEPTH:
                                dve.wait_ge(S["pair_summed"], g - DEPTH + 1)
                            dve.tensor_tensor(onehot[:, pb, :, :], iota_row[:, :].unsqueeze(1).to_broadcast([P, 2, P]),
                                              rel[:, k % 2, 2 * j:2 * j + 2].unsqueeze(2).to_broadcast([P, 2, P]),
                                              ALU.is_equal)
                            dve.wait_ge(S["hi_ready"], g + 1)
                            dve.tensor_tensor(lo[:, pb, :, :], rows[:, slot, :, :], hi[:, pb, :, :].bitcast(f32),
                                              ALU.subtract).then_inc(S["lo_ready"], 1)
                        if j == 0 and pairs:
                            window_float(t + 1)
                        if j == 1 and stage_a:
                            b = (k - 1) % 2
                            dve.wait_ge(S["pair_summed"], PAIRS * t)
                            dve.wait_ge(S["self_in"][b], 16 * (i + (k - 1) // 2 + 1))
                            if not known or t >= 2:
                                dve.wait_ge(S["agg_turned"], t - 1)
                            dve.tensor_tensor(halves(agg[:, :]), acc[:, b, :, 0:H], halves(self_row[:, b, :]),
                                              ALU.add).then_inc(S["agg_ready"], 1)
                        if j == 1 and pairs:
                            window_cols(t + 1, (k + 1) % 2)
                        if j == 5 and stage_b:
                            dve.wait_ge(S["dense_done"], t - 1)
                            w = dinv[:, ds(t - 2, 1)]
                            if l == 0:
                                if not known or t >= 3:
                                    dve.wait_ge(S["next_ready"], t - 2)
                                dve.scalar_tensor_tensor(halves(hid[:, :]), mm[:, :, 0:H], w, halves(bias_bc[0][:, :]),
                                                         ALU.mult, ALU.add).then_inc(S["scaled_ready"], 1)
                            else:
                                dve.wait_ge(S["res_biased"], t - 1)
                                xt = halves(xs[:, k % 2, :])
                                dve.scalar_tensor_tensor(xt, mm[:, :, 0:H], w, xt, ALU.mult, ALU.add
                                                         ).then_inc(S["next_ready"], 1)
                        if j == 7 and l == 1 and stage_a:
                            b = (k - 1) % 2
                            dve.wait_ge(S["res_in"][b], 16 * (i + (k - 1) // 2 + 1))
                            dve.tensor_tensor(xs[:, b, :], xs[:, b, :], bias_bc[1][:, :], ALU.add
                                              ).then_inc(S["res_biased"], 1)
                        if j == 1 and l == 1 and (not known or t >= 3):
                            read_logits(t - 3)

                def read_logits(t):
                    dve.wait_ge(S["logit_done"], t + 1)
                    dve.tensor_copy(logits[:, ds(t, 1), :], tp[:, 1, H:H + SLOTS].unsqueeze(1)
                                    ).then_inc(S["logit_read"], 1)
                layer_sweep(dve, step)
                if l == 1:
                    read_logits(T - 1)

            dve.wait_ge(L[1]["stats_done"], T)
            for b in range(2):
                dve.wait_ge(L[1]["stored"][b], done_count(b, 2))
            one.then(dve.tensor_scalar(recip_var[:, 0:T], ssq[:, :], 1.0 / D, LN_EPS, ALU.mult, ALU.add))
            one.then(dve.reciprocal(recip_var[:, 0:T], recip_var[:, 0:T]))
            one.then(dve.tensor_tensor(coef, ssq[:, :], recip_var[:, 0:T], ALU.mult))
            dve.sem_inc(F["root_in"], 1)
            dve.wait_ge(F["root_done"], 2)
            one.then(dve.tensor_scalar(coef, coef, L2_EPS, None, ALU.add))
            one.then(dve.reciprocal(coef, coef))
            one.then(dve.tensor_tensor(coef, coef, recip_var[:, 0:T], ALU.mult))
            gain = coef.unsqueeze(2).to_broadcast([P, T, SLOTS])
            one.then(dve.tensor_tensor(logits[:, :, :], logits[:, :, :], gain, ALU.mult))
            top = small[:, 0, 0:SLOTS]
            one.then(dve.tensor_reduce(top, logits[:, 0:T - 1, :].rearrange("p t q -> p q t"), AX.X, ALU.max))
            one.then(dve.tensor_tensor(top[0:LAST, :], top[0:LAST, :], logits[0:LAST, T - 1, :], ALU.max))
            dve.sem_inc(F["top_ready"], 1)
            dve.wait_ge(F["turned"], 1)
            one.then(dve.tensor_reduce(small[0:SLOTS, 1, 0:1], tp[0:SLOTS, 0, 0:P], AX.X, ALU.max))
            one.then(dve.tensor_copy(hid[0:SLOTS, 0:P], small[0:SLOTS, 1, 0:1].to_broadcast([SLOTS, P])))
            dve.sem_inc(F["top_ready"], 1)
            dve.wait_ge(F["turned"], 2)
            one.then(dve.tensor_copy(top, tp[:, 1, 0:SLOTS]))
            one.then(dve.tensor_tensor(dw[:, :, :], logits[:, :, :],
                                       top.unsqueeze(1).to_broadcast([P, T, SLOTS]), ALU.subtract))
            dve.sem_inc(F["exp_in"], 1)
            cm = small[:, 1, 0:T]
            one.then(dve.tensor_reduce(cm, logits[:, :, :], AX.X, ALU.max))
            one.then(dve.tensor_tensor(cw[:, :, :], logits[:, :, :], cm.unsqueeze(2).to_broadcast([P, T, SLOTS]),
                                       ALU.subtract))
            dve.sem_inc(F["exp_in"], 1)
            dve.wait_ge(F["exp_done"], 1)
            sumd = small[:, 2, 0:SLOTS]
            one.then(dve.tensor_reduce(sumd, dw[:, 0:T - 1, :].rearrange("p t q -> p q t"), AX.X, ALU.add))
            one.then(dve.tensor_tensor(sumd[0:LAST, :], sumd[0:LAST, :], dw[0:LAST, T - 1, :], ALU.add))
            dve.sem_inc(F["sumd_ready"], 1)
            dve.wait_ge(F["exp_done"], 2)
            one.then(dve.tensor_reduce(cm, cw[:, :, :], AX.X, ALU.add))
            one.then(dve.reciprocal(cm, cm))
            one.then(dve.tensor_tensor(cw[:, :, :], cw[:, :, :], cm.unsqueeze(2).to_broadcast([P, T, SLOTS]),
                                       ALU.mult))
            dve.sem_inc(F["c_ready"], 1)
            dve.wait_ge(F["sumd_done"], 1)
            zr = small[0:SLOTS, 3, 0:1]
            one.then(dve.reciprocal(zr, tp[0:SLOTS, 0, 0:1]))
            dve.wait_ge(F["mixed_done"], T)
            mix = agg[0:SLOTS, :]
            one.then(dve.tensor_scalar(halves(mix), mm[0:SLOTS, :, 0:H], zr, None, ALU.mult))
            mu = small[0:SLOTS, 3, 1:2]
            one.then(dve.tensor_reduce(mu, mix, AX.X, ALU.add))
            one.then(dve.tensor_scalar(mu, mu, 1.0 / D, None, ALU.mult))
            one.then(dve.tensor_scalar(mix, mix, mu, None, ALU.subtract))
            dve.sem_inc(F["mix_ready"], 1)
            dve.wait_ge(F["turned"], 3)
            mixT = aggT[:, :, 0:SLOTS]
            one.then(dve.tensor_copy(mixT, tp[:, 0, 0:KC * SLOTS].rearrange("p (k q) -> p k q", k=KC)))
            bdT = small[0:HID, 4, 0:EXPERTS]
            one.then(dve.tensor_copy(bdT, tp[0:HID, 1, 0:EXPERTS]))
            one.then(dve.tensor_copy(sel[:, :, :],
                                     ident[0:EXPERTS, 0:EXPERTS].unsqueeze(2).to_broadcast([EXPERTS, EXPERTS, SLOTS_PER])))
            dve.sem_inc(F["mixT_ready"], 1)
            dve.wait_ge(F["down_done"], 1)
            one.then(dve.tensor_tensor(hidT[:, :].rearrange("p (n q) -> p n q", n=EXPERTS),
                                       mm[0:HID, 0, 0:SLOTS].rearrange("p (n q) -> p n q", n=EXPERTS),
                                       bdT.unsqueeze(2).to_broadcast([HID, EXPERTS, SLOTS_PER]), ALU.add))
            dve.sem_inc(F["gelu_in"], 1)
            dve.wait_ge(F["up_done"], 1)
            yT = xsT[:, :, 0:SLOTS]
            one.then(dve.tensor_copy(yT, mm[:, 1, 0:KC * SLOTS].rearrange("p (k q) -> p k q", k=KC)))
            one.then(dve.tensor_copy(halves(hid[0:SLOTS, :]), acc[0:SLOTS, 0, :, 0:H]))
            dve.sem_inc(F["yT_ready"], 1)
            dve.wait_ge(F["turned"], 4)
            one.then(dve.tensor_tensor(halves(hid[0:SLOTS, :]), tp[0:SLOTS, :, 0:H], halves(hid[0:SLOTS, :]), ALU.add))
            dve.sem_inc(F["y_slots_ready"], 1)

            def add_out(i, k):
                t, b = 4 * i + k, k % 4
                dve.wait_ge(F["y_done"], t + 1)
                dve.wait_ge(fx_in[b], 16 * (i + k // 4 + 1) + done_count(b, 4))
                xt = halves(xr[:, b, :])
                dve.tensor_tensor(xt, acc[:, k % 2, :, 0:H], xt, ALU.add).then_inc(F["out_ready"], 1)
            load_sweep(dve, add_out)

        @block.tensor
        def _(pe):
            pe.wait_ge(s["ready_consts"], 1)
            for n in range(2 * KC):
                pe.wait_ge(s["w_in"][n % 2], 16 * (n // 2 + 1))
                if n:
                    pe.wait_ge(s["w_moved"], n)
                for kc in range(KC):
                    m = pe.transpose(tp[:, kc // 3, (kc % 3) * P:(kc % 3 + 1) * P],
                                     ynext[:, n % 2, kc * P:(kc + 1) * P], ident[:, :])
                m.then_inc(s["w_turned"], 1)

            def count(i, k):
                b, g = k % 2, 2 * i + k
                known = isinstance(i, int)
                pe.wait_ge(s["onehots_ready"], g + 1)
                for j in range(GROUP):
                    m = pe.matmul(mm[0:T, 0, 0:P], oh_high[0:EP, b, j, :], oh_low[0:EP, b, j, :],
                                  start=(known and g == 0 and j == 0), stop=(known and g == GROUPS - 1 and j == GROUP - 1))
                m.then_inc(s["onehots_used"], 1)
            group_sweep(pe, count)
            pe.wait_ge(s["counts_sb"], 1)
            pe.wait_ge(s["w_moved"], 2 * KC)
            pe.transpose(tp[:, 0, 0:T], hid[0:T, 0:P], ident[0:T, 0:T]).then_inc(s["degrees_done"], 1)
            pe.wait_ge(s["degrees_sb"], 1)
            pe.matmul(tp[0:1, 1, 0:TC], ones[:, 0:1], deg, start=True, stop=True)
            pe.matmul(tp[0:1, 1, 64:65], ones[0:EP, 0:1], vsum, start=True, stop=True).then_inc(s["totals_done"], 1)
            pe.wait_ge(s["slots_scaled"], 1)
            for kc in range(KC):
                m = pe.matmul(mm[:, 1, 0:SLOTS], ones[:, :], sp_c[:, kc, :], start=kc == 0, stop=kc == KC - 1)
            m.then_inc(s["slot_sums"], 1)
            pe.wait_ge(s["slots_ready"], 1)

            counts = over_counters(pe, "pe")
            for l in range(2):
                S = L[l]
                def turn_window(t):
                    pe.wait_ge(S["edges_float"], t + 1)
                    pe.matmul(tp[:, 0, H:H + 32 + CHUNKS], erow_f[0:32 + CHUNKS, :],
                              ident[0:32 + CHUNKS, 0:32 + CHUNKS], start=True, stop=True
                              ).then_inc(S["edges_turned"], 1)
                turn_window(0)
                over_pe(pe, l, *counts)

                def dense(parts):
                    for part in parts:
                        kc, h = divmod(part, 2)
                        m = pe.matmul(mm[:, h, 0:H], aggT[:, kc, :], WT[l][:, kc, h * H:(h + 1) * H],
                                      start=kc == 0, stop=kc == KC - 1)
                    return m

                def step(i, k):
                    t = 2 * i + k
                    known = isinstance(i, int)
                    pairs, stage_a, stage_b = (not known or t < T), (not known or 1 <= t <= T), (not known or t >= 2)
                    for j in range(PAIRS):
                        if pairs:
                            g, pb = PAIRS * t + j, (PAIRS * k + j) % DEPTH
                            if j == 0 and (not known or t >= 2):
                                pe.wait_ge(S["agg_ready"], t - 1)
                            pe.wait_ge(S["lo_ready"], g + 1)
                            for c in range(2):
                                for part in (hi, lo):
                                    for h in range(2):
                                        m = pe.matmul(acc[:, k % 2, h, 0:H], onehot[:, pb, c, :],
                                                      part[:, pb, c, h * H:(h + 1) * H],
                                                      start=(j == 0 and c == 0 and part is hi),
                                                      stop=(j == PAIRS - 1 and c == 1 and part is lo))
                            m.then_inc(S["pair_summed"], 1)
                        if j == 0 and pairs:
                            if not known or t >= 2:
                                pe.wait_ge(S["aggT_ready"], t - 1)
                            turn_window(t + 1)
                        if j == 2 and stage_a:
                            pe.wait_ge(S["agg_ready"], t)
                            if pairs:
                                pe.wait_ge(S["idx_ready"], t + 2)
                            if l == 1 and (not known or t >= 3):
                                pe.wait_ge(S["logit_read"], t - 2)
                            for kc in range(KC):
                                m = pe.transpose(tp[:, kc // 3, (kc % 3) * P:(kc % 3 + 1) * P],
                                                 agg[:, kc * P:(kc + 1) * P], ident[:, :])
                            m.then_inc(S["agg_turned"], 1)
                        if j >= 5 and stage_a:
                            if j == 5:
                                pe.wait_ge(S["aggT_ready"], t)
                                if not known or t >= 2:
                                    pe.wait_ge(S["scaled_ready" if l == 0 else "next_ready"], t - 1)
                            dense(range(3 * (j - 5) // 2, 3 * (j - 4) // 2))
                        if j < 4 and stage_b:
                            m = dense(range(3 * (j + 4) // 2, 3 * (j + 5) // 2))
                            if j == 3:
                                m.then_inc(S["dense_done"], 1)
                        if j == 6 and l == 1 and stage_b:
                            pe.wait_ge(S["next_ready"], t - 1)
                            for kc in range(KC):
                                m = pe.transpose(tp[:, kc // 3, (kc % 3) * P:(kc % 3 + 1) * P],
                                                 xs[:, k % 2, kc * P:(kc + 1) * P], ident[:, :])
                            m.then_inc(S["x_turned"], 1)
                        if j == 8 and l == 1 and stage_b:
                            pe.wait_ge(S["xT_ready"], t - 1)
                            for kc in range(KC):
                                m = pe.matmul(tp[:, 1, H:H + SLOTS], xsT[:, kc, :], sp_c[:, kc, :],
                                              start=kc == 0, stop=kc == KC - 1)
                            m.then_inc(S["logit_done"], 1)
                layer_sweep(pe, step)

            pe.wait_ge(F["top_ready"], 1)
            pe.transpose(tp[0:SLOTS, 0, 0:P], small[:, 0, 0:SLOTS], ident[:, :]).then_inc(F["turned"], 1)
            pe.wait_ge(F["top_ready"], 2)
            pe.matmul(tp[:, 1, 0:SLOTS], hid[0:SLOTS, 0:P], ident[0:SLOTS, 0:SLOTS], start=True, stop=True
                      ).then_inc(F["turned"], 1)
            pe.wait_ge(F["sumd_ready"], 1)
            pe.matmul(tp[0:SLOTS, 0, 0:1], small[:, 2, 0:SLOTS], ones[:, 0:1], start=True, stop=True
                      ).then_inc(F["sumd_done"], 1)

            def mix_tile(i, k):
                t, b = 4 * i + k, k % 4
                n = full(i, k, t)
                first, last = (isinstance(i, int) and t == 0), (isinstance(i, int) and t == T - 1)
                pe.wait_ge(F["w_staged"], t + 1)
                pe.wait_ge(fx_in[b], 16 * (i + k // 4 + 1))
                for h in range(2):
                    m = pe.matmul(mm[0:SLOTS, h, 0:H], w_tile[0:n, b, :],
                                  xr[0:n, b, h * H:(h + 1) * H], start=first, stop=last)
                m.then_inc(F["mixed_done"], 1)
            load_sweep(pe, mix_tile)
            pe.wait_ge(F["mix_ready"], 1)
            pe.wait_ge(F["w_in"], 16 * (EXPERTS + 3))
            for kc in range(KC):
                pe.transpose(tp[:, 0, kc * SLOTS:(kc + 1) * SLOTS], agg[0:SLOTS, kc * P:(kc + 1) * P],
                             ident[0:SLOTS, 0:SLOTS])
            pe.transpose(tp[0:HID, 1, 0:EXPERTS], bdown[:, :], ident[0:EXPERTS, 0:EXPERTS]).then_inc(F["turned"], 1)
            pe.wait_ge(F["mixT_ready"], 1)
            for n in range(EXPERTS):
                q = slice(n * SLOTS_PER, (n + 1) * SLOTS_PER)
                for kc in range(KC):
                    m = pe.matmul(mm[0:HID, 0, q], wdown[:, kc, n, :], aggT[:, kc, q], start=kc == 0, stop=kc == KC - 1)
            m.then_inc(F["down_done"], 1)
            pe.wait_ge(F["gelu_done"], 1)
            for kc in range(KC):
                for n in range(EXPERTS):
                    q0 = kc * SLOTS + n * SLOTS_PER
                    pe.matmul(mm[:, 1, q0:q0 + SLOTS_PER], wup[:, n, kc * P:(kc + 1) * P],
                              hidT[:, n * SLOTS_PER:(n + 1) * SLOTS_PER], start=True, stop=True)
            for h in range(2):
                m = pe.matmul(acc[0:SLOTS, 0, h, 0:H], sel[:, :, :].rearrange("p n q -> p (n q)"),
                              bup[:, h * H:(h + 1) * H], start=True, stop=True)
            m.then_inc(F["up_done"], 1)
            pe.wait_ge(F["yT_ready"], 1)
            for kc in range(KC):
                m = pe.transpose(tp[0:SLOTS, kc // 3, (kc % 3) * P:(kc % 3 + 1) * P], xsT[:, kc, 0:SLOTS], ident[:, :])
            m.then_inc(F["turned"], 1)
            pe.wait_ge(F["y_slots_ready"], 1)

            def turn_c(t, b):
                pe.wait_ge(F["c_staged"], t + 1)
                pe.transpose(tp[0:SLOTS, b, 0:P], c_tile[:, b, :], ident[:, :]).then_inc(F["c_turned"], 1)
            turn_c(0, 0)

            def out_tile(i, k):
                t, b = 4 * i + k, k % 2
                known = isinstance(i, int)
                if not (known and t == T - 1):
                    if t != 0 if known else True:
                        pe.wait_ge(F["c_moved"], t)
                    turn_c(t + 1, (k + 1) % 2)
                pe.wait_ge(F["c_moved"], t + 1)
                if k >= 2 or not known:
                    pe.wait_ge(F["out_ready"], t - 1)
                for h in range(2):
                    m = pe.matmul(acc[:, b, h, 0:H], cT[:, b, :], hid[0:SLOTS, h * H:(h + 1) * H],
                                  start=True, stop=True)
                m.then_inc(F["y_done"], 1)
            load_sweep(pe, out_tile)


_NAMES = {"x": "x", "src": "src", "dst": "dst", "W1": "L0_gnn_W1", "b1": "L0_gnn_b1", "W2": "L0_gnn_W2",
          "b2": "L0_gnn_b2", "slots": "L0_ffn_slot_params", "scale": "L0_ffn_scale", "W_down": "L0_ffn_W_down",
          "b_down": "L0_ffn_b_down", "W_up": "L0_ffn_W_up", "b_up": "L0_ffn_b_up"}


def kernel(**inputs):
    import concourse.bacc as bacc
    from concourse import mybir
    from concourse.bass_utils import run_bass_kernel_spmd as run

    nc = bacc.Bacc("TRN2", target_bir_lowering=False, num_devices=1)
    arrays, aps = {}, {}
    for short, name in _NAMES.items():
        v = np.ascontiguousarray(inputs[name])
        if v.ndim == 0:
            v = v.reshape(1)
        arrays["in_" + short] = v
        aps[short] = nc.dram_tensor("in_" + short, v.shape, mybir.dt.from_np(v.dtype), kind="ExternalInput").ap()
    aps["out"] = nc.dram_tensor("out_x", (N, D), mybir.dt.float32, kind="ExternalOutput").ap()
    build(nc, aps)
    return run(nc, [arrays], core_ids=[0]).results[0]["out_x"]
```
